# Optimizing a Trainium2 kernel written in Bass

```python
import numpy as np
import jax
import jax.numpy as jnp

def _softmax(x, axis=-1):
    return jax.nn.softmax(x, axis=axis)

def _gelu(x):
    return jax.nn.gelu(x, approximate=True)

def _silu(x):
    return jax.nn.silu(x)

def _sigmoid(x):
    return jax.nn.sigmoid(x)

def _layernorm(x, axis=-1, eps=1e-05):
    m = jnp.mean(x, axis=axis, keepdims=True)
    v = jnp.var(x, axis=axis, keepdims=True)
    return (x - m) / jnp.sqrt(v + eps)

def _scatter_add(tgt, idx, src, axis=0):
    return tgt.at[idx].add(src)

def _segment_sum(src, seg, n):
    return jax.ops.segment_sum(src, seg, n)
kernel_name = 'mk_gnn_preln_d2_gnn_r8_4e2f96'

def setup_inputs(seed: int=0):
    np.random.seed(seed)
    _w = jnp.asarray

    def _rec_inputs():
        import jax
        import jax.numpy as jnp
        _gk = jax.random.key(seed)
        x = -0.000202 + 1 * jax.random.normal(jax.random.fold_in(_gk, 1), (12500, 64), jnp.float32)
        src = jax.random.randint(jax.random.fold_in(_gk, 2), (400000,), 0, 12500, jnp.int32)
        dst = jax.random.randint(jax.random.fold_in(_gk, 3), (400000,), 0, 12500, jnp.int32)
        _o = jnp.argsort(dst, stable=True)
        src = src[_o]
        dst = dst[_o]
        edge_attr_32 = -8.62073e-06 + 0.999901 * jax.random.normal(jax.random.fold_in(_gk, 11), (400000, 32), jnp.float32)
        return (x, src, dst, edge_attr_32)
    x, src, dst, edge_attr_32 = _rec_inputs()

    def _L0_gnn_setup():
        import jax, jax.numpy as jnp
        import numpy as np
        N_NODES = 12500
        N_EDGES = 125000
        NODE_DIM = 64
        EDGE_DIM = 32
        EPS = 1e-05
        SLOPE = 0.1

        def _mlp2(v, W1, b1, W2, b2):
            h = jax.nn.leaky_relu(v @ W1 + b1, negative_slope=SLOPE)
            return h @ W2 + b2
        key = jax.random.key(seed)
        ks = jax.random.split(key, 8)
        s = 0.05
        return {'x': jax.random.normal(ks[0], (N_NODES, NODE_DIM), dtype=jnp.float32), 'edge_attr': jax.random.normal(ks[1], (N_EDGES, EDGE_DIM), dtype=jnp.float32), 'W1n': jax.random.normal(ks[2], (NODE_DIM, 2 * NODE_DIM), dtype=jnp.float32) * s, 'b1n': jnp.zeros((2 * NODE_DIM,), dtype=jnp.float32), 'W2n': jax.random.normal(ks[3], (2 * NODE_DIM, NODE_DIM), dtype=jnp.float32) * s, 'b2n': jnp.zeros((NODE_DIM,), dtype=jnp.float32), 'W1e': jax.random.normal(ks[4], (EDGE_DIM, NODE_DIM), dtype=jnp.float32) * s, 'b1e': jnp.zeros((NODE_DIM,), dtype=jnp.float32), 'W2e': jax.random.normal(ks[5], (NODE_DIM, NODE_DIM), dtype=jnp.float32) * s, 'b2e': jnp.zeros((NODE_DIM,), dtype=jnp.float32), 'res_w': jnp.ones((1,), dtype=jnp.float32), 'dp_scale': jnp.ones((1,), dtype=jnp.float32), 'gamma': jnp.ones((NODE_DIM,), dtype=jnp.float32), 'beta': jnp.zeros((NODE_DIM,), dtype=jnp.float32), 'edge_index': jax.random.randint(ks[6], (2, N_EDGES), 0, N_NODES, dtype=jnp.int64) if jax.config.jax_enable_x64 else jax.random.randint(ks[6], (2, N_EDGES), 0, N_NODES, dtype=jnp.int32)}
    _L0_gnn_all = _L0_gnn_setup()
    _L0_gnn_in = {k: v for k, v in _L0_gnn_all.items() if k in ('W1n', 'b1n', 'W2n', 'b2n', 'W1e', 'b1e', 'W2e', 'b2e', 'res_w', 'dp_scale', 'gamma', 'beta')}
    del _L0_gnn_all

    def _L1_gnn_setup():
        import jax, jax.numpy as jnp
        import numpy as np
        N_NODES = 12500
        N_EDGES = 200000
        IN_CH = 64
        OUT_CH = 64
        key = jax.random.key(seed)
        ks = jax.random.split(key, 6)
        x = jax.random.normal(ks[0], (N_NODES, IN_CH), dtype=jnp.float32)
        edge_index = jax.random.randint(ks[1], (2, N_EDGES), 0, N_NODES, dtype=jnp.int64)
        W1 = jax.random.normal(ks[2], (2 * IN_CH, OUT_CH), dtype=jnp.float32) * (1.0 / np.sqrt(2 * IN_CH))
        b1 = jnp.zeros((OUT_CH,), dtype=jnp.float32)
        W2 = jax.random.normal(ks[3], (OUT_CH, OUT_CH), dtype=jnp.float32) * (1.0 / np.sqrt(OUT_CH))
        b2 = jnp.zeros((OUT_CH,), dtype=jnp.float32)
        return {'x': x, 'edge_index': edge_index, 'W1': W1, 'b1': b1, 'W2': W2, 'b2': b2}
    _L1_gnn_all = _L1_gnn_setup()
    _L1_gnn_in = {k: v for k, v in _L1_gnn_all.items() if k in ('W1', 'b1', 'W2', 'b2')}
    del _L1_gnn_all
    return {'x': x, 'src': src, 'dst': dst, 'edge_attr_32': edge_attr_32, 'L0_gnn_W1n': _L0_gnn_in['W1n'], 'L0_gnn_b1n': _L0_gnn_in['b1n'], 'L0_gnn_W2n': _L0_gnn_in['W2n'], 'L0_gnn_b2n': _L0_gnn_in['b2n'], 'L0_gnn_W1e': _L0_gnn_in['W1e'], 'L0_gnn_b1e': _L0_gnn_in['b1e'], 'L0_gnn_W2e': _L0_gnn_in['W2e'], 'L0_gnn_b2e': _L0_gnn_in['b2e'], 'L0_gnn_res_w': _L0_gnn_in['res_w'], 'L0_gnn_dp_scale': _L0_gnn_in['dp_scale'], 'L0_gnn_gamma': _L0_gnn_in['gamma'], 'L0_gnn_beta': _L0_gnn_in['beta'], 'L1_gnn_W1': _L1_gnn_in['W1'], 'L1_gnn_b1': _L1_gnn_in['b1'], 'L1_gnn_W2': _L1_gnn_in['W2'], 'L1_gnn_b2': _L1_gnn_in['b2']}

def reference(x, src, dst, edge_attr_32, L0_gnn_W1n, L0_gnn_b1n, L0_gnn_W2n, L0_gnn_b2n, L0_gnn_W1e, L0_gnn_b1e, L0_gnn_W2e, L0_gnn_b2e, L0_gnn_res_w, L0_gnn_dp_scale, L0_gnn_gamma, L0_gnn_beta, L1_gnn_W1, L1_gnn_b1, L1_gnn_W2, L1_gnn_b2):
    import jax
    import jax.numpy as jnp

    def _L0_gnn_ref(x, edge_attr, W1n, b1n, W2n, b2n, W1e, b1e, W2e, b2e, res_w, dp_scale, gamma, beta, edge_index):
        import jax, jax.numpy as jnp
        import numpy as np
        N_NODES = 12500
        N_EDGES = 125000
        NODE_DIM = 64
        EDGE_DIM = 32
        EPS = 1e-05
        SLOPE = 0.1

        def _mlp2(v, W1, b1, W2, b2):
            h = jax.nn.leaky_relu(v @ W1 + b1, negative_slope=SLOPE)
            return h @ W2 + b2
        num_nodes = x.shape[0]
        x_t = _mlp2(x, W1n, b1n, W2n, b2n)
        e_t = _mlp2(edge_attr, W1e, b1e, W2e, b2e)
        src, dst = (edge_index[0], edge_index[1])
        msgs = x_t[src] * e_t * dp_scale
        aggregated = jax.ops.segment_sum(msgs, dst, num_segments=num_nodes)
        out = x + aggregated * res_w
        mu = jnp.mean(out, axis=-1, keepdims=True)
        var = jnp.mean(jnp.square(out - mu), axis=-1, keepdims=True)
        return (out - mu) * jax.lax.rsqrt(var + EPS) * gamma + beta

    def _L1_gnn_ref(x, edge_index, W1, b1, W2, b2):
        import jax, jax.numpy as jnp
        import numpy as np
        N_NODES = 12500
        N_EDGES = 200000
        IN_CH = 64
        OUT_CH = 64
        src = edge_index[0]
        dst = edge_index[1]
        x_i = x[dst]
        x_j = x[src]
        edge_features = jnp.concatenate([x_i, x_j - x_i], axis=-1)
        h = jax.nn.relu(edge_features @ W1 + b1)
        edge_messages = h @ W2 + b2
        out = jax.ops.segment_max(edge_messages, dst, num_segments=x.shape[0])
        return jnp.where(jnp.isfinite(out), out, jnp.zeros_like(out))
    edge_index = jnp.stack([src, dst])
    h = jnp.maximum(_layernorm(x, axis=-1), 0.0)
    x = x + _L0_gnn_ref(h, edge_attr_32, L0_gnn_W1n, L0_gnn_b1n, L0_gnn_W2n, L0_gnn_b2n, L0_gnn_W1e, L0_gnn_b1e, L0_gnn_W2e, L0_gnn_b2e, L0_gnn_res_w, L0_gnn_dp_scale, L0_gnn_gamma, L0_gnn_beta, edge_index)
    h = jnp.maximum(_layernorm(x, axis=-1), 0.0)
    x = x + _L1_gnn_ref(h, edge_index, L1_gnn_W1, L1_gnn_b1, L1_gnn_W2, L1_gnn_b2)
    return x

_drawn_inputs = setup_inputs


def setup_inputs(seed=0):
    import zlib

    import numpy as np

    out = dict(_drawn_inputs(seed))
    spreads = {'L0_gnn_b1n': (0.0, 0.1),
     'L0_gnn_b2n': (0.0, 0.1),
     'L0_gnn_b1e': (0.0, 0.1),
     'L0_gnn_b2e': (0.0, 0.1),
     'L0_gnn_gamma': (1.0, 0.2),
     'L0_gnn_beta': (0.0, 0.1),
     'L1_gnn_b1': (0.0, 0.282),
     'L1_gnn_b2': (0.0, 0.1)}
    factors = {}
    for name, (base, spread) in spreads.items():
        noise = np.random.default_rng([zlib.crc32(name.encode()), seed]).standard_normal(out[name].shape)
        drawn = base * np.exp(spread * noise) if base else spread * noise
        out[name] = jnp.asarray(drawn.astype(out[name].dtype))
    for name, factor in factors.items():
        out[name] = (out[name] * factor).astype(out[name].dtype)
    return out
```

```python
from contextlib import ExitStack

import concourse.bass as bass
from concourse import mybir

F32 = mybir.dt.float32
BF16 = mybir.dt.bfloat16
I32 = mybir.dt.int32
U32 = mybir.dt.uint32
ALU = mybir.AluOpType
ACT = mybir.ActivationFunctionType
AX_X = mybir.AxisListType.X

P = 128
SC = 512
J = SC // P
NP = 125
CH = 20
GB = 4
EPS = 1e-5
SLOPE = 0.1
ROUND = 12582912.0
BIG = 3.3895313892515355e38
FLT_MAX = 3.4028234663852886e38


def stream_sizes(n_edges):
    tiles = -(-n_edges // (2 * SC))
    return tiles, tiles * SC


def build(nc, x, src_streams, dst, attr_streams, W1n, b1n, W2n, b2n, W1e, b1e, W2e, b2e,
          res_w, dp_scale, gamma, beta, W1, b1, W2, b2, out):
    N, D = x.shape
    E = dst.shape[0]
    EA = W1e.shape[0]
    HN = W1n.shape[1]
    ST, SE = stream_sizes(E)
    SEAM = E - SE
    ROW1 = 1 - 2 * SEAM
    NC = N // NP
    NCH = NC // CH
    NG = NC // GB
    GPC = CH // GB
    HC = E // P
    HT = 2 * J
    H_LAST = HC - HT * (ST - 1)
    assert NC * NP == N and NC % CH == 0 and CH == 5 * GB and HC * P == E
    assert D == 64 and EA == 32 and HN == 128 and ST % 2 == 1 and ST >= 5 and 0 < H_LAST <= HT
    assert NC <= 128 and 2 * SE + N < 2 ** 24

    node_table = nc.dram_tensor("node_table", (N, D), F32, kind="Internal").ap()
    node_table1 = nc.dram_tensor("node_table1", (N, D), F32, kind="Internal").ap()
    scan_rows = nc.dram_tensor("scan_rows", (2 * SE, D), F32, kind="Internal").ap()
    scan_rows1 = nc.dram_tensor("scan_rows1", (2 * SE, D), F32, kind="Internal").ap()
    first_rows = nc.dram_tensor("first_rows", (2 * SE + N, D), F32, kind="Internal").ap()
    same_row = nc.dram_tensor("same_row", (E,), BF16, kind="Internal").ap()

    with ExitStack() as ctx:
        ctx.enter_context(nc.allow_non_contiguous_dma(reason="columns of constants"))

        def sb(name, shape, dt=F32):
            return ctx.enter_context(nc.sbuf_tensor(name, shape, dt))

        def sem(name):
            return ctx.enter_context(nc.semaphore(name))

        def sems(name, n=2):
            return [sem(f"{name}_{i}") for i in range(n)]

        psum = ctx.enter_context(nc.psum_tensor("psum", [P, 8, SC], F32))
        bank = [psum[:, i, :] for i in range(8)]

        x_sb = sb("x_sb", [NP, NC * D])
        h_sb = sb("h_sb", [NP, NC * D])
        agg_sb = sb("agg_sb", [NP, NC * D])
        first_sb = sb("first_sb", [P, NC * D])
        sq_sb = sb("sq_sb", [NP, CH * D])
        stat_sum = sb("stat_sum", [NP, CH])
        stat_sd = sb("stat_sd", [NP, CH])
        hT_sb = [sb(f"hT_sb{i}", [P, 2 * NP]) for i in range(2)]
        hid_n_sb = [sb(f"hid_n_sb{i}", [P, GB * NP]) for i in range(2)]
        dst_sb = first_sb[:, 0:HC].bitcast(I32)
        quot_sb = first_sb[:, HC:2 * HC]
        prev_sb = sb("prev_sb", [P, 1], I32)
        same_sb = sb("same_sb", [P, HC], BF16)
        hi_sb = sb("hi_sb", [P, HC], BF16)
        lo_sb = sb("lo_sb", [P, HC], BF16)
        idx_all = sb("idx_all", [P, (ST + 2) * HT], I32)
        iota_i = sb("iota_i", [P, P], I32)
        iota_b = sb("iota_b", [P, P], BF16)
        node_id_i = sb("node_id_i", [NP, NC], I32)
        hot_hi = sb("hot_hi", [P, HT, NP], BF16)
        hot_lo = sb("hot_lo", [P, HT, NC], BF16)
        counts = sb("counts", [NP, NC])
        plan = sb("plan", [NP, 10, NC])
        ends_plan, starts_plan, in1_plan, any_plan, span_plan, coef_plan, low_plan, t0_plan, t1_plan, ones_plan = \
            [plan[:, i, :] for i in range(10)]
        row_sum = sb("row_sum", [NP, 1])
        before_sb = sb("before_sb", [NP, 1])
        last_idx = sb("last_idx", [NP, NC], I32)
        first_idx = sb("first_idx", [NP, NC], I32)
        seam_row = sb("seam_row", [NP, D])
        seam_row1 = sb("seam_row1", [NP, D])
        held_row = sb("held_row", [1, P])
        held_init = sb("held_init", [P, 1])
        ident = sb("ident", [P, P])
        before = sb("before", [NP, NP])
        sel01 = sb("sel01", [3, 2, D], BF16)
        sel_lim = sb("sel_lim", [3, 2, D], BF16)
        one_sb = sb("one_sb", [1, 1])
        eps_sb = sb("eps_sb", [P, 1])
        zeros = sb("zeros", [P, SC])
        W1n_sb = sb("W1n_sb", [P, HN])
        W2n_sb = sb("W2n_sb", [HN, D])
        W1e_sb = sb("W1e_sb", [2 * EA, P])
        W2e_sb = sb("W2e_sb", [P, P])
        W2_sb = sb("W2_sb", [P, P])
        Wab_sb = sb("Wab_sb", [P, 2 * D])
        b1n_sb = sb("b1n_sb", [P, 1])
        b1e_sb = sb("b1e_sb", [P, 1])
        b2e_sb = sb("b2e_sb", [P, 1])
        b2_sb = sb("b2_sb", [P, 1])
        b2n_row = sb("b2n_row", [NP, D])
        b1_row = sb("b1_row", [NP, D])
        gamma_row = sb("gamma_row", [NP, D])
        beta_row = sb("beta_row", [NP, D])
        scales = sb("scales", [NP, 2])
        idx_sb = [sb(f"idx_sb{i}", [P, HT], I32) for i in range(2)]
        got_sb = [sb(f"got_sb{i}", [P, J * 2 * D]) for i in range(2)]
        attr_sb = [sb(f"attr_sb{i}", [2 * EA, SC]) for i in range(2)]
        seg_sb = [sb(f"seg_sb{i}", [3, SC], BF16) for i in range(2)]
        run_sb = [sb(f"run_sb{i}", [P, SC]) for i in range(2)]
        rows_sb = [sb(f"rows_sb{i}", [P, 2 * J * D]) for i in range(2)]
        held_in = [sb(f"held_in{i}", [P, 2 * J * D]) for i in range(2)]
        held_sb = [sb(f"held_sb{i}", [P, SC]) for i in range(2)]
        hid_sb = sb("hid_sb", [P, SC])
        eT_sb = sb("eT_sb", [P, SC])
        msg_sb = sb("msg_sb", [P, SC])
        aT_sb = eT_sb
        pre_sb = hid_sb
        act_sb = sb("act_sb", [P, SC])

        node_const_in = sem("node_const_in")
        const_in, dst_in, idx_in = sem("const_in"), sem("dst_in"), sem("idx_in")
        x_in = sems("x_in", NCH)
        pool_ready, dve_ready, weights_ready = sem("pool_ready"), sem("dve_ready"), sem("weights_ready")
        pool_step, pool_const = sem("pool_step"), sem("pool_const")
        prep_step, same_stored = sem("prep_step"), sem("same_stored")
        n0_dve, n0_act = sem("n0_dve"), sem("n0_act")
        n0_tp, n0_hT, n0_mm1, n0_lin, n0_hid, n0_mm2, n0_xt = [sem("n0_" + s) for s in ("tp", "hT", "mm1", "lin", "hid", "mm2", "xt")]
        table_stored, table1_stored = sem("table_stored"), sem("table1_stored")
        idx_ready = sem("idx_ready")
        attr_in, seg_in, got_in, stored = sems("attr_in"), sems("seg_in"), sems("got_in"), sems("stored")
        zeroed = sem("zeroed")
        hid_lin = sem("hid_lin")
        hid_mm, hid_ready, e_mm, e_ready, mask_done = [sem(s) for s in ("hid_mm", "hid_ready", "e_mm", "e_ready", "mask_done")]
        xT_done, msg_done, run_done, back_done, rows_ready = [sem(s) for s in ("xT_done", "msg_done", "run_done", "back_done", "rows_ready")]
        hot_ready, hist_mm, hist_added = sem("hot_ready"), sem("hist_mm"), sem("hist_added")
        plan_step, before_mm, before_ready = sem("plan_step"), sem("before_mm"), sem("before_ready")
        seam_in, seam1_in = sem("seam_in"), sem("seam1_in")
        ext_in, ext1_in = sems("ext_in", NCH), sems("ext1_in", NCH)
        n1_dve, n1_act = sem("n1_dve"), sem("n1_act")
        n1_tp, n1_hT, n1_mm, n1_first, n1_src, n1_span = [sem("n1_" + s) for s in ("tp", "hT", "mm", "first", "src", "span")]
        scattered, held_row_ready, held_mm, held_init_ready = [sem(s) for s in ("scattered", "held_row_ready", "held_mm", "held_init_ready")]
        idx1_ready = sem("idx1_ready")
        seg1_in, held_rows_in, got1_in, stored1 = sems("seg1_in"), sems("held_rows_in"), sems("got1_in"), sems("stored1")
        m01_done, lim_done, aT_done, aT_ready, held_done = [sem(s) for s in ("m01_done", "lim_done", "aT_done", "aT_ready", "held_done")]
        bT_done, pre_done, act_done, m_mm, m_ready = [sem(s) for s in ("bT_done", "pre_done", "act_done", "m_mm", "m_ready")]
        run1_done, back1_done, rows1_ready = sem("run1_done"), sem("back1_done"), sem("rows1_ready")
        n2_dve, out_stored = sem("n2_dve"), sem("out_stored")

        K0D, K0A = 7, 2

        def since(count, first):
            return not isinstance(count, int) or count >= first

        def supertiles(eng, body):
            body(0, 0, 0)
            body(1, 0, 1)
            with eng.Fori(1, ST // 2) as i:
                body(i * 2, i, 0)
                body(i * 2 + 1, i, 1)
            body(ST - 1, ST // 2, 0, True)

        def blocks(t, c0, n=CH):
            return t[0:NP, c0 * D:(c0 + n) * D].rearrange("p (c d) -> p c d", d=D)

        def over_d(col, c0):
            return col[:, c0:c0 + CH].unsqueeze(2).broadcast_to((NP, CH, D))

        def over_c(row, n=CH):
            return row[:, :].unsqueeze(1).broadcast_to((NP, n, D))

        def edge_order(ps):
            return ps[:, :].rearrange("f (j p) -> f p j", j=J)

        def products(q):
            b = 2 + 2 * (q % 2)
            return psum[0:NP, b:b + 2, 0:4 * D].rearrange("p h (i w) -> p h i w", i=2)

        def by_half(t, q):
            return t[0:NP, q * GB * D:(q + 1) * GB * D].rearrange("p (i h d) -> p h i d", i=2, h=2)

        def node_view(table):
            return table.rearrange("(p c) d -> p (c d)", p=NP)

        def tile_rows(table, t):
            return table[bass.ds(t * (2 * SC), 2 * SC), :].rearrange("(p j) d -> p (j d)", p=P)

        block = ctx.enter_context(nc.Block())

        @block.sync
        def _(sp):
            for ch in range(NCH):
                cols = slice(ch * CH * D, (ch + 1) * CH * D)
                for a, b in ((0, 112), (112, NP)):
                    sp.dma_start(x_sb[a:b, cols], node_view(x)[a:b, cols]).then_inc(x_in[ch], 16)
            sp.wait_ge(dve_ready, 1)
            sp.dma_start(dst_sb, dst.rearrange("(p c) -> p c", p=P)).then_inc(dst_in, 16)
            sp.dma_start(prev_sb[1:P, :], dst.rearrange("(p c) -> p c", p=P)[0:P - 1, HC - 1:HC]).then_inc(dst_in, 16)
            sp.dma_start(idx_all[:, 0:ST * HT], src_streams).then_inc(idx_in, 16)
            def const(dst_ap, src_ap):
                sp.dma_start(dst_ap, src_ap).then_inc(const_in, 16)

            def column(v):
                return v.rearrange("(n a) -> n a", a=1)

            sp.wait_ge(dve_ready, 2)
            for s in range(2):
                const(W1e_sb[s * EA:(s + 1) * EA, s * D:(s + 1) * D], W1e)
                const(W2e_sb[s * D:(s + 1) * D, s * D:(s + 1) * D], W2e)
                const(b1e_sb[s * D:(s + 1) * D, :], column(b1e))
                const(b2e_sb[s * D:(s + 1) * D, :], column(b2e))
                const(W2_sb[s * D:(s + 1) * D, s * D:(s + 1) * D], W2)
                const(b2_sb[s * D:(s + 1) * D, :], column(b2))
                const(Wab_sb[s * D:(s + 1) * D, 0:D], W1[0:D, :])
            for s in range(2):
                const(Wab_sb[s * D:(s + 1) * D, D:2 * D], W1[D:2 * D, :])
            const(b1_row[:, :], b1.partition_broadcast(NP))
            const(gamma_row[:, :], gamma.partition_broadcast(NP))
            const(beta_row[:, :], beta.partition_broadcast(NP))
            const(scales[:, 0:1], res_w.partition_broadcast(NP))
            const(scales[:, 1:2], dp_scale.partition_broadcast(NP))
            sp.wait_ge(prep_step, 2)
            sp.dma_start(same_row.rearrange("(p c) -> p c", p=P), same_sb[:, :]).then_inc(same_stored, 16)
            for ch in range(NCH):
                sp.wait_ge(n0_xt, (ch + 1) * GPC)
                cols = slice(ch * CH * D, (ch + 1) * CH * D)
                for a, b in ((0, 112), (112, NP)):
                    sp.dma_start(node_view(node_table)[a:b, cols], agg_sb[a:b, cols]).then_inc(table_stored, 16)
            sp.wait_ge(same_stored, 16)
            sp.wait_ge(pool_const, 1)

            def load(t, u, k):
                if since(t, 2):
                    sp.wait_ge(hid_mm, t - 1)
                    sp.nop(nofuse=True)
                sp.dma_start(attr_sb[k][:, :], attr_streams[:, bass.ds(t * SC, SC)]).then_inc(attr_in[k], 16)
                if since(t, 2):
                    sp.wait_ge(mask_done, t - 1)
                    sp.nop(nofuse=True)
                for s in range(2):
                    sp.dma_start(seg_sb[k][s:s + 1, :], same_row[bass.ds(t * SC + s * SEAM, SC)].rearrange("(a n) -> a n", a=1)).then_inc(seg_in[k], 16)

            def store(t, u, k):
                sp.dma_start(tile_rows(first_rows, t), zeros[:, :]).then_inc(zeroed, 16)
                sp.wait_ge(rows_ready, t + 1)
                sp.nop(nofuse=True)
                sp.dma_start(tile_rows(scan_rows, t), rows_sb[k][:, :]).then_inc(stored[k], 16)

            load(0, 0, 0)
            load(1, 0, 1)
            load(2, 1, 0)
            store(0, 0, 0)
            with sp.Fori(1, ST // 2) as i:
                load(i * 2 + 1, i, 1)
                store(i * 2 - 1, i - 1, 1)
                load(i * 2 + 2, i + 1, 0)
                store(i * 2, i, 0)
            store(ST - 2, ST // 2 - 1, 1)
            store(ST - 1, ST // 2, 0)

            sp.wait_ge(stored[0], 16 * (ST // 2 + 1))
            sp.wait_ge(stored[1], 16 * (ST // 2))
            sp.dma_start(seam_row[:, :], scan_rows[2 * (SEAM - 1), :].partition_broadcast(NP)).then_inc(seam_in, 16)
            for ch in range(NCH):
                sp.wait_ge(n1_src, (ch + 1) * GPC)
                cols = slice(ch * CH * D, (ch + 1) * CH * D)
                for a, b in ((0, 112), (112, NP)):
                    sp.dma_start(node_view(node_table1)[a:b, cols], agg_sb[a:b, cols]).then_inc(table1_stored, 16)
            sp.wait_ge(scattered, NC * 16)

            def load1(t, u, k):
                if since(t, 2):
                    sp.wait_ge(lim_done, t - 1)
                    sp.nop(nofuse=True)
                for s in range(2):
                    sp.dma_start(seg_sb[k][s:s + 1, :], same_row[bass.ds(t * SC + s * SEAM, SC)].rearrange("(a n) -> a n", a=1)).then_inc(seg1_in[k], 16)
                if since(t, 2):
                    sp.wait_ge(aT_done, t - 1)
                    sp.nop(nofuse=True)
                sp.dma_start(held_in[k][:, :], tile_rows(first_rows, t)).then_inc(held_rows_in[k], 16)

            def store1(t, u, k):
                sp.wait_ge(rows1_ready, t + 1)
                sp.nop(nofuse=True)
                sp.dma_start(tile_rows(scan_rows1, t), rows_sb[k][:, :]).then_inc(stored1[k], 16)

            load1(0, 0, 0)
            load1(1, 0, 1)
            load1(2, 1, 0)
            store1(0, 0, 0)
            with sp.Fori(1, ST // 2) as i:
                load1(i * 2 + 1, i, 1)
                store1(i * 2 - 1, i - 1, 1)
                load1(i * 2 + 2, i + 1, 0)
                store1(i * 2, i, 0)
            store1(ST - 2, ST // 2 - 1, 1)
            store1(ST - 1, ST // 2, 0)

            sp.wait_ge(stored1[0], 16 * (ST // 2 + 1))
            sp.wait_ge(stored1[1], 16 * (ST // 2))
            sp.dma_start(seam_row1[:, :], scan_rows1[2 * (SEAM - 1), :].partition_broadcast(NP)).then_inc(seam1_in, 16)
            for ch in range(NCH):
                sp.wait_ge(n2_dve, (ch + 1) * K2D)
                cols = slice(ch * CH * D, (ch + 1) * CH * D)
                for a, b in ((0, 112), (112, NP)):
                    sp.dma_start(node_view(out)[a:b, cols], h_sb[a:b, cols]).then_inc(out_stored, 16)
            sp.wait_ge(out_stored, 32 * NCH)

        @block.gpsimd
        def _(pool):
            pool.memset(ident[:, :], 0.0).then_inc(pool_step, 1)
            pool.memset(before[:, :], 1.0).then_inc(pool_step, 1)
            pool.memset(sel01[:, :, :], 0.0).then_inc(pool_step, 1)
            pool.memset(sel_lim[:, :, :], 0.0).then_inc(pool_step, 1)
            pool.iota(iota_i[:, :], [[1, P]], base=0, channel_multiplier=0).then_inc(pool_step, 1)
            pool.iota(node_id_i[:, :], [[1, NC]], base=0, channel_multiplier=NC).then_inc(pool_step, 1)
            pool.wait_ge(pool_step, 4)
            pool.affine_select(out=ident[:, :], in_=ident[:, :], compare_op=ALU.not_equal, fill=1.0, base=0,
                               pattern=[[-1, P]], channel_multiplier=1).then_inc(pool_ready, 1)
            pool.affine_select(out=before[:, :], in_=before[:, :], compare_op=ALU.is_gt, fill=0.0, base=0,
                               pattern=[[1, NP]], channel_multiplier=-1).then_inc(pool_ready, 1)
            pool.affine_select(out=sel01[:, :, :], in_=sel01[:, :, :], compare_op=ALU.not_equal, fill=0.5, base=0,
                               pattern=[[-1, 2], [0, D]], channel_multiplier=1).then_inc(pool_step, 1)
            pool.wait_ge(pool_step, 7)
            pool.affine_select(out=sel01[:, :, :], in_=sel01[:, :, :], compare_op=ALU.not_equal, fill=0.5, base=-2,
                               pattern=[[0, 2], [0, D]], channel_multiplier=1).then_inc(pool_ready, 1)
            pool.affine_select(out=sel_lim[:, :, :], in_=sel_lim[:, :, :], compare_op=ALU.not_equal, fill=BIG, base=0,
                               pattern=[[-1, 2], [0, D]], channel_multiplier=1).then_inc(pool_ready, 1)
            pool.memset(zeros[:, :], 0.0).then_inc(pool_const, 1)
            pool.wait_ge(table_stored, 32 * NCH)

            def gather(table, ready, used, landed, t, k):
                pool.wait_ge(ready, t + 1)
                if since(t, 2):
                    pool.wait_ge(used, t - 1)
                pool.nop(nofuse=True)
                for j in range(J):
                    for s in range(2):
                        pool.indirect_dma_start(
                            got_sb[k][:, (2 * j + s) * D:(2 * j + s + 1) * D], None, table,
                            bass.IndirectOffsetOnAxis(ap=idx_sb[k][:, s * J + j:s * J + j + 1].bitcast(U32), axis=0)
                        ).then_inc(landed[k], 16)

            supertiles(pool, lambda t, u, k, last=False: gather(node_table, idx_ready, xT_done, got_in, t, k))

            pool.wait_ge(plan_step, LAST_IDX_STEP)
            pool.wait_ge(stored[0], 16 * (ST // 2 + 1))
            pool.wait_ge(stored[1], 16 * (ST // 2))
            pool.wait_ge(table_stored, 32 * NCH)
            for c in range(NC):
                pool.indirect_dma_start(agg_sb[:, c * D:(c + 1) * D], None, scan_rows,
                                        bass.IndirectOffsetOnAxis(ap=last_idx[:, c:c + 1].bitcast(U32), axis=0)
                                        ).then_inc(ext_in[c // CH], 16)
            pool.wait_ge(zeroed, 16 * ST)
            pool.wait_ge(plan_step, PLAN_STEPS)
            for c in range(NC):
                pool.wait_ge(n1_first, c // GB + 1)
                pool.indirect_dma_start(first_rows, bass.IndirectOffsetOnAxis(ap=first_idx[:, c:c + 1].bitcast(U32), axis=0),
                                        first_sb[0:NP, c * D:(c + 1) * D], None).then_inc(scattered, 16)
            pool.wait_ge(table1_stored, 32 * NCH)
            supertiles(pool, lambda t, u, k, last=False: gather(node_table1, idx1_ready, bT_done, got1_in, t, k))
            pool.wait_ge(stored1[0], 16 * (ST // 2 + 1))
            pool.wait_ge(stored1[1], 16 * (ST // 2))
            for c in range(NC):
                pool.indirect_dma_start(agg_sb[:, c * D:(c + 1) * D], None, scan_rows1,
                                        bass.IndirectOffsetOnAxis(ap=last_idx[:, c:c + 1].bitcast(U32), axis=0)
                                        ).then_inc(ext1_in[c // CH], 16)

        @block.scalar
        def _(act):
            def const(dst_ap, src_ap):
                act.dma_start(dst_ap, src_ap).then_inc(node_const_in, 16)

            const(W1n_sb[0:D, :], W1n)
            const(W1n_sb[D:P, :], W1n)
            const(W2n_sb[:, :], W2n)
            const(b1n_sb[:, :], b1n.rearrange("(n a) -> n a", a=1))
            const(b2n_row[:, :], b2n.partition_broadcast(NP))

            def deviation(dve_sem, d0, act_sem):
                act.wait_ge(dve_sem, d0 + 5)
                act.activation(stat_sd[:, :], stat_sum[:, :], ACT.Sqrt, bias=eps_sb[0:NP, :], scale=1.0 / D).then_inc(act_sem, 1)

            def relu_chunk(ch, dve_sem, d0, act_sem):
                act.wait_ge(dve_sem, d0 + 7)
                act.activation(blocks(h_sb, ch * CH), blocks(h_sb, ch * CH), ACT.Relu).then_inc(act_sem, 1)

            def hT_copy(q, tp, mm, hT):
                act.wait_ge(tp, q + 1)
                if q >= 2:
                    act.wait_ge(mm, q - 1)
                act.activation(hT_sb[q % 2][:, :], bank[q % 2][:, 0:2 * NP], ACT.Copy).then_inc(hT, 1)

            def n0_group(q):
                hT_copy(q, n0_tp, n0_mm1, n0_hT)
                act.wait_ge(n0_mm1, q + 1)
                if q >= 2:
                    act.wait_ge(n0_mm2, q - 1)
                b = 2 + 2 * (q % 2)
                act.activation(hid_n_sb[q % 2][:, :].rearrange("h (e n) -> h e n", e=2), psum[:, b:b + 2, 0:2 * NP],
                               ACT.Identity, bias=b1n_sb[:, :]).then_inc(n0_lin, 1)

            act.wait_ge(dve_ready, 3)
            for step in range(NCH + 2):
                if step == 2:
                    act.wait_ge(node_const_in, 16 * N_NODE_CONSTS)
                for g in range(GPC):
                    if step >= 2:
                        n0_group((step - 2) * GPC + g)
                    if step < NCH and g == 1:
                        deviation(n0_dve, K0D * step, n0_act)
                    if step < NCH and g == 2:
                        relu_chunk(step, n0_dve, K0D * step, n0_act)

            def rows_copy(t, u, k, back, store_sem, ready):
                act.wait_ge(back, t + 1)
                if since(u, 1):
                    act.wait_ge(store_sem[k], u * 16)
                act.activation(rows_sb[k][:, :], bank[6][:, :], ACT.Copy).then_inc(ready, 1)

            def edge_mlp(t):
                act.wait_ge(hid_mm, t + 1)
                if since(t, 1):
                    act.wait_ge(e_mm, t)
                act.activation(hid_sb[:, :], bank[0][:, :], ACT.Identity, bias=b1e_sb[:, :]).then_inc(hid_lin, 1)
                act.wait_ge(e_mm, t + 1)
                if since(t, 1):
                    act.wait_ge(msg_done, t)
                act.activation(eT_sb[:, :], bank[1][:, :], ACT.Identity, bias=b2e_sb[:, :]).then_inc(e_ready, 1)

            def layer0(t, u, k, last=False):
                if since(t, 1):
                    rows_copy(t - 1, u + k - 1, 1 - k, back_done, stored, rows_ready)
                if not last:
                    edge_mlp(t + 1)

            act.wait_ge(const_in, 16 * N_CONSTS)
            edge_mlp(0)
            supertiles(act, layer0)
            rows_copy(ST - 1, ST // 2, 0, back_done, stored, rows_ready)

            act.wait_ge(before_mm, 1)
            act.activation(before_sb[:, :], bank[7][0:NP, 0:1], ACT.Copy).then_inc(before_ready, 1)

            def n1_source(q):
                act.wait_ge(n1_first, q + 1)
                act.activation(by_half(agg_sb, q), products(q)[:, :, :, D:2 * D], ACT.Copy).then_inc(n1_src, 1)

            for ch in range(NCH + 1):
                d0 = K1D * ch
                for g in range(GPC):
                    if ch:
                        q = (ch - 1) * GPC + g
                        hT_copy(q, n1_tp, n1_mm, n1_hT)
                        if q:
                            n1_source(q - 1)
                    if ch < NCH and g == 1:
                        deviation(n1_dve, d0 + N1_LN0, n1_act)
                    if ch < NCH and g == 3:
                        deviation(n1_dve, d0 + N1_LN1, n1_act)
                    if ch < NCH and g == 4:
                        relu_chunk(ch, n1_dve, d0 + N1_LN1, n1_act)
            n1_source(NG - 1)
            act.wait_ge(n1_span, 1)
            act.wait_ge(dve_ready, 4)
            act.activation(held_row[0:1, D:P], bank[7][0:1, 0:D], ACT.Copy).then_inc(held_row_ready, 1)
            act.wait_ge(held_mm, 1)
            act.activation(held_init[:, :], bank[5][:, 0:1], ACT.Copy).then_inc(held_init_ready, 1)

            def a_copy(t):
                act.wait_ge(aT_done, t + 1)
                if since(t, 1):
                    act.wait_ge(held_done, t)
                act.activation(aT_sb[:, :].rearrange("f (p j) -> f p j", j=J), edge_order(bank[4]), ACT.Copy).then_inc(aT_ready, 1)

            def layer1(t, u, k, last=False):
                act.wait_ge(pre_done, t + 1)
                if since(t, 1):
                    act.wait_ge(m_mm, t)
                act.activation(act_sb[:, :], pre_sb[:, :], ACT.Relu).then_inc(act_done, 1)
                if since(t, 1):
                    rows_copy(t - 1, u + k - 1, 1 - k, back1_done, stored1, rows1_ready)
                if not last:
                    a_copy(t + 1)
                act.wait_ge(m_mm, t + 1)
                if since(t, 1):
                    act.wait_ge(run1_done, t)
                act.activation(msg_sb[:, :], bank[5][:, :], ACT.Identity, bias=b2_sb[:, :]).then_inc(m_ready, 1)

            a_copy(0)
            supertiles(act, layer1)
            rows_copy(ST - 1, ST // 2, 0, back1_done, stored1, rows1_ready)

        @block.tensor
        def _(pe):
            pe.wait_ge(pool_ready, 4)
            pe.wait_ge(node_const_in, 16 * N_NODE_CONSTS)

            def transposes(q, h_ready, h_count, hT, tp):
                pe.wait_ge(h_ready, h_count)
                if q >= 2:
                    pe.wait_ge(hT, q - 1)
                for i in range(2):
                    c = q * GB + 2 * i
                    last = pe.transpose(bank[q % 2][:, i * NP:(i + 1) * NP], h_sb[:, c * D:(c + 2) * D], ident[0:NP, 0:NP])
                last.then_inc(tp, 1)

            def n0_first(q):
                pe.wait_ge(n0_hT, q + 1)
                if q >= 2:
                    pe.wait_ge(n0_lin, q - 1)
                for half in range(2):
                    last = pe.matmul(bank[2 + 2 * (q % 2) + half][:, 0:2 * NP], W1n_sb[half * D:(half + 1) * D, :],
                                     hT_sb[q % 2][half * D:(half + 1) * D, :], start=True, stop=True)
                last.then_inc(n0_mm1, 1)

            def n0_second(q):
                pe.wait_ge(n0_hid, q + 1)
                if q >= 2:
                    pe.wait_ge(n0_xt, q - 1)
                for c in range(GB):
                    at = (c % 2) * 2 * NP + (c // 2) * NP
                    last = pe.matmul(bank[6 + q % 2][0:NP, c * D:(c + 1) * D], hid_n_sb[q % 2][:, at:at + NP], W2n_sb[:, :],
                                     start=True, stop=True)
                last.then_inc(n0_mm2, 1)

            for q in range(NG + 2):
                if q < NG:
                    transposes(q, n0_act, K0A * (q // GPC + 1), n0_hT, n0_tp)
                if 0 < q <= NG:
                    n0_first(q - 1)
                if q > 1:
                    n0_second(q - 2)
            pe.wait_ge(const_in, 16 * N_CONSTS)
            pe.wait_ge(n0_lin, NG)
            pe.wait_ge(n0_xt, NG)

            def mask(sel, b, k):
                return pe.matmul(bank[b][:, :], sel[:, :, :].rearrange("r s d -> r (s d)"), seg_sb[k][:, :], start=True, stop=True)

            def transpose_rows(b, rows):
                for j in range(J):
                    last = pe.transpose(bank[b][:, j * P:(j + 1) * P], rows(j), ident[:, :])
                return last

            def gathered(k):
                return lambda j: got_sb[k][:, j * P:(j + 1) * P]

            def scanned(k):
                return lambda j: run_sb[k][:, :].rearrange("f (p j) -> f p j", j=J)[:, :, j]

            def histogram(t, n):
                pe.wait_ge(hot_ready, t * 2 + 2)
                if since(t, 1):
                    pe.wait_ge(hist_added, t)
                for c in range(n):
                    last = pe.matmul(bank[5][0:NP, 0:NC], hot_hi[:, c, :], hot_lo[:, c, :], start=(c == 0), stop=(c == n - 1))
                last.then_inc(hist_mm, 1)

            def edge_mlp(t, u, k):
                pe.wait_ge(attr_in[k], u * 16 + 16)
                if since(t, 1):
                    pe.wait_ge(hid_lin, t)
                pe.matmul(bank[0][:, :], W1e_sb[:, :], attr_sb[k][:, :], start=True, stop=True).then_inc(hid_mm, 1)
                pe.wait_ge(hid_ready, t + 1)
                if since(t, 1):
                    pe.wait_ge(e_ready, t)
                pe.matmul(bank[1][:, :], W2e_sb[:, :], hid_sb[:, :], start=True, stop=True).then_inc(e_mm, 1)

            def back(t, k, run, rows, done):
                pe.wait_ge(run, t + 1)
                if since(t, 1):
                    pe.wait_ge(rows, t)
                transpose_rows(6, scanned(k)).then_inc(done, 1)

            def layer0(t, u, k, last=False):
                pe.wait_ge(got_in[k], u * (HT * 16) + HT * 16)
                if since(t, 2):
                    pe.wait_ge(msg_done, t - 1)
                transpose_rows(2 + k, gathered(k)).then_inc(xT_done, 1)
                if since(t, 1):
                    back(t - 1, 1 - k, run_done, rows_ready, back_done)
                pe.wait_ge(seg_in[k], u * 32 + 32)
                if since(t, 1):
                    pe.wait_ge(run_done, t)
                mask(sel01, 4, k).then_inc(mask_done, 1)
                if not last:
                    edge_mlp(t + 1, u + k, 1 - k)
                histogram(t, H_LAST if last else HT)

            edge_mlp(0, 0, 0)
            supertiles(pe, layer0)
            back(ST - 1, 0, run_done, rows_ready, back_done)

            pe.wait_ge(plan_step, 1)
            pe.matmul(bank[7][0:NP, 0:1], before[:, :], row_sum[:, :], start=True, stop=True).then_inc(before_mm, 1)
            pe.wait_ge(rows_ready, ST)
            pe.wait_ge(before_ready, 1)

            def n1_products(q):
                pe.wait_ge(n1_hT, q + 1)
                if q >= 2:
                    pe.wait_ge(n1_first, q - 1)
                if q >= 2:
                    pe.wait_ge(n1_src, q - 1)
                for c in range(GB):
                    half = c % 2
                    last = pe.matmul(bank[2 + 2 * (q % 2) + half][0:NP, (c // 2) * 2 * D:(c // 2 + 1) * 2 * D],
                                     hT_sb[q % 2][half * D:(half + 1) * D, (c // 2) * NP:(c // 2 + 1) * NP],
                                     Wab_sb[half * D:(half + 1) * D, :], start=True, stop=True)
                last.then_inc(n1_mm, 1)

            def n1_seam(q):
                pe.wait_ge(n1_first, q + 1)
                for c in range(q * GB, (q + 1) * GB):
                    last = pe.matmul(bank[7][0:1, 0:D], span_plan[:, c:c + 1], first_sb[0:NP, c * D:(c + 1) * D],
                                     start=(c == 0), stop=(c == NC - 1))
                return last

            pe.wait_ge(plan_step, PLAN_STEPS)
            pe.wait_ge(weights_ready, 1)
            for q in range(NG + 2):
                if 0 < q <= NG and q % GPC == 0:
                    n1_products(q - 1)
                if q < NG:
                    transposes(q, n1_act, K1A * (q // GPC + 1), n1_hT, n1_tp)
                if 0 < q <= NG and q % GPC != 0:
                    n1_products(q - 1)
                if q > 1:
                    last = n1_seam(q - 2)
            last.then_inc(n1_span, 1)
            pe.wait_ge(held_row_ready, 1)
            pe.wait_ge(dve_ready, 4)
            pe.matmul(bank[5][:, 0:1], held_row[:, :], one_sb[:, :], start=True, stop=True).then_inc(held_mm, 1)
            pe.wait_ge(held_init_ready, 1)
            pe.wait_ge(n1_first, NG)
            pe.wait_ge(n1_src, NG)

            def held_part(t, u, k):
                pe.wait_ge(seg1_in[k], u * 32 + 32)
                if since(t, 1):
                    pe.wait_ge(held_done, t)
                mask(sel01, 0, k).then_inc(m01_done, 1)
                pe.wait_ge(held_rows_in[k], u * 16 + 16)
                if since(t, 1):
                    pe.wait_ge(aT_ready, t)
                transpose_rows(4, lambda j: held_in[k][:, j * P:(j + 1) * P]).then_inc(aT_done, 1)

            def layer1(t, u, k, last=False):
                pe.wait_ge(got1_in[k], u * (HT * 16) + HT * 16)
                if since(t, 2):
                    pe.wait_ge(pre_done, t - 1)
                transpose_rows(2 + k, gathered(k)).then_inc(bT_done, 1)
                if since(t, 1):
                    back(t - 1, 1 - k, run1_done, rows1_ready, back1_done)
                if since(t, 1):
                    pe.wait_ge(run1_done, t)
                mask(sel_lim, 1, k).then_inc(lim_done, 1)
                if not last:
                    held_part(t + 1, u + k, 1 - k)
                pe.wait_ge(act_done, t + 1)
                if since(t, 1):
                    pe.wait_ge(m_ready, t)
                pe.matmul(bank[5][:, :], W2_sb[:, :], act_sb[:, :], start=True, stop=True).then_inc(m_mm, 1)

            held_part(0, 0, 0)
            supertiles(pe, layer1)
            back(ST - 1, 0, run1_done, rows1_ready, back1_done)

        @block.vector
        def _(dve):
            V = nc.vector
            V.memset(prev_sb[:, :], -1)
            V.memset(idx_all[:, ST * HT:(ST + 2) * HT], 0).then_inc(dve_ready, 1)
            V.memset(W1e_sb[:, :], 0.0)
            V.memset(W2e_sb[:, :], 0.0)
            V.memset(W2_sb[:, :], 0.0).then_inc(dve_ready, 1)
            V.memset(eps_sb[:, :], EPS).then_inc(dve_ready, 1)
            V.memset(ones_plan, 1.0)
            V.memset(one_sb[:, :], 1.0)
            V.memset(held_row[:, :], 0.0)
            V.memset(counts[:, :], 0.0)
            for k in range(2):
                last = V.memset(seg_sb[k][:, :], 1.0)
            last.then_inc(dve_ready, 1)


            def norm_chunk(ch, src_blocks, dve_sem, act_sem, kd, d0, ka, a0, beside):
                hc = blocks(h_sb, ch * CH)
                D0, A0 = kd * ch + d0, ka * ch + a0
                V.tensor_reduce(stat_sum[:, :], src_blocks, AX_X, ALU.add).then_inc(dve_sem, 1)
                dve.wait_ge(dve_sem, D0 + 1)
                V.tensor_scalar(stat_sum[:, :], stat_sum[:, :], 1.0 / D, None, ALU.mult).then_inc(dve_sem, 1)
                dve.wait_ge(dve_sem, D0 + 2)
                V.tensor_tensor(hc, src_blocks, over_d(stat_sum, 0), ALU.subtract).then_inc(dve_sem, 1)
                dve.wait_ge(dve_sem, D0 + 3)
                V.tensor_tensor(blocks(sq_sb, 0), hc, hc, ALU.mult).then_inc(dve_sem, 1)
                beside()
                dve.wait_ge(dve_sem, D0 + 4)
                V.tensor_reduce(stat_sum[:, :], blocks(sq_sb, 0), AX_X, ALU.add).then_inc(dve_sem, 1)
                dve.wait_ge(act_sem, A0 + 1)
                V.reciprocal(stat_sd[:, :], stat_sd[:, :]).then_inc(dve_sem, 1)
                dve.wait_ge(dve_sem, D0 + 6)
                V.tensor_tensor(hc, hc, over_d(stat_sd, 0), ALU.mult).then_inc(dve_sem, 1)

            def leaky(t, ready):
                V.scalar_tensor_tensor(t[:, :], t[:, :], SLOPE, t[:, :], ALU.mult, ALU.max).then_inc(ready, 1)

            def n0_hidden(q):
                dve.wait_ge(n0_lin, q + 1)
                leaky(hid_n_sb[q % 2], n0_hid)

            def n0_rows(q):
                dve.wait_ge(n0_mm2, q + 1)
                V.tensor_tensor(blocks(agg_sb, q * GB, GB), bank[6 + q % 2][0:NP, 0:GB * D].rearrange("p (c d) -> p c d", d=D),
                                over_c(b2n_row, GB), ALU.add).then_inc(n0_xt, 1)

            dve.wait_ge(node_const_in, 16 * N_NODE_CONSTS)

            def n0_group(step, g):
                if step >= 2:
                    q = (step - 2) * GPC + g
                    n0_hidden(q)
                    if q:
                        n0_rows(q - 1)

            def prepare(n):
                if n == 0:
                    dve.wait_ge(const_in, 16 * N_CONSTS)
                    V.tensor_tensor(Wab_sb[:, 0:D], Wab_sb[:, 0:D], Wab_sb[:, D:2 * D], ALU.subtract).then_inc(weights_ready, 1)
                    dve.wait_ge(pool_step, 6)
                    V.tensor_copy(iota_b[:, :], iota_i[:, :])
                    dve.wait_ge(dst_in, 32)
                    V.tensor_tensor(same_sb[:, 1:HC], dst_sb[:, 1:HC], dst_sb[:, 0:HC - 1], ALU.is_equal)
                    V.tensor_tensor(same_sb[:, 0:1], dst_sb[:, 0:1], prev_sb[:, :], ALU.is_equal).then_inc(prep_step, 1)
                if n == 1:
                    dve.wait_ge(prep_step, 1)
                    V.tensor_scalar(same_sb[:, :], same_sb[:, :], 2.0, -1.0, ALU.mult, ALU.add).then_inc(prep_step, 1)
                    V.tensor_scalar(quot_sb, dst_sb, 1.0 / NC, -(NC - 1) / (2.0 * NC), ALU.mult, ALU.add).then_inc(prep_step, 1)
                    dve.wait_ge(prep_step, 3)
                    V.tensor_scalar(quot_sb, quot_sb, ROUND, ROUND, ALU.add, ALU.subtract).then_inc(prep_step, 1)
                    dve.wait_ge(prep_step, 4)
                    V.tensor_copy(hi_sb[:, :], quot_sb).then_inc(prep_step, 1)
                    V.scalar_tensor_tensor(lo_sb[:, :], quot_sb, -float(NC), dst_sb, ALU.mult, ALU.add).then_inc(prep_step, 1)

            for step in range(NCH + 2):
                n0_group(step, 0)
                if step < NCH:
                    dve.wait_ge(x_in[step], 32)
                    norm_chunk(step, blocks(x_sb, step * CH), n0_dve, n0_act, K0D, 0, K0A, 0, lambda: n0_group(step, 1))
                else:
                    n0_group(step, 1)
                for g in range(2, GPC):
                    n0_group(step, g)
                    if g == 3 and step >= 2:
                        prepare(step - 2)
            n0_rows(NG - 1)
            dve.wait_ge(idx_in, 16)

            def copy_idx(t, k, ready):
                V.tensor_copy(idx_sb[k][:, :], idx_all[:, bass.ds(t * HT, HT)]).then_inc(ready, 1)

            copy_idx(0, 0, idx_ready)
            copy_idx(1, 1, idx_ready)
            dve.wait_ge(prep_step, 6)

            def one_hot(out_t, col, t, n, width):
                V.tensor_tensor(out_t[:, 0:n, :], iota_b[:, 0:width].unsqueeze(1).broadcast_to((P, n, width)),
                                col[:, bass.ds(t * HT, n)].unsqueeze(2).broadcast_to((P, n, width)), ALU.is_equal).then_inc(hot_ready, 1)

            def edge_hidden(t):
                dve.wait_ge(hid_lin, t + 1)
                leaky(hid_sb, hid_ready)

            def layer0(t, u, k, last=False):
                dve.wait_ge(xT_done, t + 1)
                dve.wait_ge(e_ready, t + 1)
                V.tensor_tensor(msg_sb[:, :].rearrange("f (p j) -> f p j", j=J), eT_sb[:, :].rearrange("f (p j) -> f p j", j=J),
                                edge_order(bank[2 + k]), ALU.mult).then_inc(msg_done, 1)
                copy_idx(t + 2, k, idx_ready)
                dve.wait_ge(mask_done, t + 1)
                dve.wait_ge(msg_done, t + 1)
                if since(t, 2):
                    dve.wait_ge(back_done, t - 1)
                if since(t, 1):
                    dve.wait_ge(run_done, t)
                start = run_sb[1 - k][:, SC - 1:SC] if since(t, 1) else 0.0
                V.tensor_tensor_scan(run_sb[k][:, :], bank[4][:, :], msg_sb[:, :], start, ALU.mult, ALU.add).then_inc(run_done, 1)
                if not last:
                    edge_hidden(t + 1)
                n = H_LAST if last else HT
                if since(t, 1):
                    dve.wait_ge(hist_mm, t)
                one_hot(hot_hi, hi_sb, t, n, NP)
                one_hot(hot_lo, lo_sb, t, n, NC)
                dve.wait_ge(hist_mm, t + 1)
                if since(t, 1):
                    dve.wait_ge(hist_added, t)
                V.tensor_tensor(counts[:, :], counts[:, :], bank[5][0:NP, 0:NC], ALU.add).then_inc(hist_added, 1)

            edge_hidden(0)
            supertiles(dve, layer0)

            steps = [0]

            def step(ins):
                steps[0] += 1
                ins.then_inc(plan_step, 1)
                dve.wait_ge(plan_step, steps[0])

            dve.wait_ge(hist_added, ST)
            step(V.tensor_reduce(row_sum[:, :], counts[:, :], AX_X, ALU.add))
            dve.wait_ge(before_ready, 1)
            step(V.tensor_tensor_scan(ends_plan, ones_plan, counts[:, :], before_sb[:, :], ALU.mult, ALU.add))
            step(V.tensor_scalar(in1_plan, ends_plan, float(SEAM + 1), float(ROW1), ALU.is_ge, ALU.mult))
            step(V.tensor_scalar(t0_plan, ends_plan, 2.0, -2.0, ALU.mult, ALU.add))
            step(V.tensor_tensor(t0_plan, t0_plan, in1_plan, ALU.add))
            step(V.tensor_scalar(last_idx[:, :], t0_plan, 0.0, None, ALU.max))
            assert steps[0] == LAST_IDX_STEP
            step(V.tensor_scalar(any_plan, counts[:, :], 1.0, None, ALU.min))
            step(V.tensor_tensor(starts_plan, ends_plan, counts[:, :], ALU.subtract))
            step(V.tensor_scalar(t0_plan, starts_plan, float(SEAM), float(ROW1), ALU.is_ge, ALU.mult))
            step(V.scalar_tensor_tensor(t0_plan, starts_plan, 2.0, t0_plan, ALU.mult, ALU.add))
            step(V.tensor_scalar(t1_plan, node_id_i[:, :], float(2 * SE), None, ALU.add))
            step(V.tensor_tensor(t0_plan, t0_plan, t1_plan, ALU.subtract))
            step(V.tensor_tensor(t0_plan, t0_plan, any_plan, ALU.mult))
            step(V.tensor_tensor(first_idx[:, :], t0_plan, t1_plan, ALU.add))
            step(V.tensor_scalar(t0_plan, starts_plan, float(SEAM), None, ALU.is_lt))
            step(V.tensor_scalar(t1_plan, ends_plan, float(SEAM), None, ALU.is_gt))
            step(V.tensor_tensor(span_plan, t0_plan, t1_plan, ALU.mult))
            step(V.tensor_scalar(low_plan, span_plan, -1.0, BIG, ALU.add, ALU.mult))
            step(V.tensor_scalar(coef_plan, any_plan, scales[:, 0:1], scales[:, 1:2], ALU.mult, ALU.mult))
            assert steps[0] == PLAN_STEPS

            def n1_group(ch, g):
                if ch:
                    n1_firsts((ch - 1) * GPC + g)

            def n1_firsts(q):
                dve.wait_ge(n1_mm, q + 1)
                V.tensor_tensor(by_half(first_sb, q), products(q)[:, :, :, 0:D],
                                b1_row[:, :].unsqueeze(1).unsqueeze(1).broadcast_to((NP, 2, 2, D)), ALU.add).then_inc(n1_first, 1)

            dve.wait_ge(seam_in, 16)
            for ch in range(NCH + 1):
                if ch < NCH:
                    c0 = ch * CH
                    n1_count = [K1D * ch]

                    def link(ins):
                        n1_count[0] += 1
                        ins.then_inc(n1_dve, 1)
                        dve.wait_ge(n1_dve, n1_count[0])

                    ag, hc, xc = blocks(agg_sb, c0), blocks(h_sb, c0), blocks(x_sb, c0)
                    link(V.tensor_tensor(blocks(sq_sb, 0), over_d(span_plan, c0), over_c(seam_row), ALU.mult))
                    dve.wait_ge(ext_in[ch], CH * 16)
                    link(V.tensor_tensor(ag, ag, blocks(sq_sb, 0), ALU.add))
                    link(V.tensor_tensor(ag, ag, over_d(coef_plan, c0), ALU.mult))
                    link(V.tensor_tensor(ag, ag, hc, ALU.add))
                    n1_group(ch, 0)
                    norm_chunk(ch, ag, n1_dve, n1_act, K1D, N1_LN0, K1A, 0, lambda: n1_group(ch, 1))
                    dve.wait_ge(n1_dve, K1D * ch + N1_LN0 + 7)
                    n1_count[0] += 7
                    link(V.tensor_tensor(hc, hc, over_c(gamma_row), ALU.mult))
                    n1_group(ch, 2)
                    link(V.tensor_tensor(hc, hc, over_c(beta_row), ALU.add))
                    link(V.tensor_tensor(xc, xc, hc, ALU.add))
                    norm_chunk(ch, xc, n1_dve, n1_act, K1D, N1_LN1, K1A, 1, lambda: n1_group(ch, 3))
                    n1_group(ch, 4)
                    n1_count[0] += 7
                    assert n1_count[0] == K1D * (ch + 1)
                else:
                    for g in range(GPC):
                        n1_group(ch, g)
            copy_idx(0, 0, idx1_ready)
            copy_idx(1, 1, idx1_ready)
            dve.wait_ge(held_init_ready, 1)

            def hold(t, k):
                dve.wait_ge(aT_ready, t + 1)
                dve.wait_ge(m01_done, t + 1)
                if since(t, 2):
                    dve.wait_ge(pre_done, t - 1)
                if since(t, 1):
                    dve.wait_ge(held_done, t)
                start = held_sb[1 - k][:, SC - 1:SC] if since(t, 1) else held_init[:, :]
                V.tensor_tensor_scan(held_sb[k][:, :], bank[0][:, :], aT_sb[:, :], start, ALU.mult, ALU.add).then_inc(held_done, 1)

            def layer1(t, u, k, last=False):
                dve.wait_ge(bT_done, t + 1)
                dve.wait_ge(held_done, t + 1)
                if since(t, 1):
                    dve.wait_ge(act_done, t)
                V.tensor_tensor(pre_sb[:, :].rearrange("f (p j) -> f p j", j=J), held_sb[k][:, :].rearrange("f (p j) -> f p j", j=J),
                                edge_order(bank[2 + k]), ALU.add).then_inc(pre_done, 1)
                copy_idx(t + 2, k, idx1_ready)
                if not last:
                    hold(t + 1, 1 - k)
                dve.wait_ge(m_ready, t + 1)
                dve.wait_ge(lim_done, t + 1)
                if since(t, 2):
                    dve.wait_ge(back1_done, t - 1)
                if since(t, 1):
                    dve.wait_ge(run1_done, t)
                start = run_sb[1 - k][:, SC - 1:SC] if since(t, 1) else -FLT_MAX
                V.tensor_tensor_scan(run_sb[k][:, :], bank[1][:, :], msg_sb[:, :], start, ALU.min, ALU.max).then_inc(run1_done, 1)

            hold(0, 0)
            supertiles(dve, layer1)

            dve.wait_ge(seam1_in, 16)
            for ch in range(NCH):
                c0 = ch * CH
                n2_count = [K2D * ch]

                def link2(ins):
                    n2_count[0] += 1
                    ins.then_inc(n2_dve, 1)
                    dve.wait_ge(n2_dve, n2_count[0])

                ag, hc, xc, sq = blocks(agg_sb, c0), blocks(h_sb, c0), blocks(x_sb, c0), blocks(sq_sb, 0)
                link2(V.tensor_tensor(sq, over_d(span_plan, c0), over_c(seam_row1), ALU.mult))
                link2(V.tensor_tensor(sq, sq, over_d(low_plan, c0), ALU.add))
                link2(V.memset(hc, 0.0))
                dve.wait_ge(ext1_in[ch], CH * 16)
                link2(V.tensor_tensor(ag, ag, sq, ALU.max))
                link2(V.tensor_scalar(sq, ag, FLT_MAX, None, ALU.is_le))
                link2(V.scalar_tensor_tensor(sq, ag, -FLT_MAX, sq, ALU.is_ge, ALU.mult))
                link2(V.tensor_tensor(sq, sq, over_d(any_plan, c0), ALU.mult))
                link2(V.copy_predicated(hc, sq.bitcast(U32), ag))
                link2(V.tensor_tensor(hc, hc, xc, ALU.add))
                assert n2_count[0] == K2D * (ch + 1)


N_NODE_CONSTS, N_CONSTS = 5, 21
LAST_IDX_STEP = 6
PLAN_STEPS = 19
N1_LN0, N1_LN1 = 4, 14
K1D, K1A = 21, 3
K2D = 9


def kernel(**inputs):
    import numpy as _np
    import concourse.bacc as _bacc
    from concourse import mybir as _mybir
    from concourse.bass_utils import run_bass_kernel_spmd as _run

    src, dst, attr = (_np.asarray(inputs[n]) for n in ("src", "dst", "edge_attr_32"))
    n_edges = dst.shape[0]
    tiles, length = stream_sizes(n_edges)
    seam = n_edges - length
    src_streams = _np.stack([src[:length], src[seam:]]).reshape(2, tiles, P, J).transpose(2, 1, 0, 3).reshape(P, -1)
    attr_streams = _np.concatenate([attr[:length].T, attr[seam:].T])
    host = {"x": inputs["x"], "src_streams": src_streams, "dst": dst, "attr_streams": attr_streams}
    for name in ("W1n", "b1n", "W2n", "b2n", "W1e", "b1e", "W2e", "b2e", "res_w", "dp_scale", "gamma", "beta"):
        host[name] = inputs["L0_gnn_" + name]
    for name in ("W1", "b1", "W2", "b2"):
        host[name] = inputs["L1_gnn_" + name]
    nc = _bacc.Bacc("TRN2", target_bir_lowering=False, num_devices=1)
    arrays, args = {}, []
    for name, a in host.items():
        a = _np.ascontiguousarray(a)
        arrays[f"in_{name}"] = a
        args.append(nc.dram_tensor(f"in_{name}", a.shape, _mybir.dt.from_np(a.dtype), kind="ExternalInput").ap())
    shape = _np.asarray(inputs["x"]).shape
    result = nc.dram_tensor("result", shape, _mybir.dt.float32, kind="ExternalOutput").ap()
    build(nc, *args, result)
    return _run(nc, [arrays], core_ids=[0]).results[0]["result"]
```
